# Optimizing a Trainium2 kernel written in Bass

```python
import numpy as np
import jax
import jax.numpy as jnp

def _softmax(x, axis=-1):
    return jax.nn.softmax(x, axis=axis)
def _gelu(x):
    return jax.nn.gelu(x, approximate=True)
def _silu(x):
    return jax.nn.silu(x)
def _sigmoid(x):
    return jax.nn.sigmoid(x)
def _layernorm(x, axis=-1, eps=1e-5):
    m = jnp.mean(x, axis=axis, keepdims=True)
    v = jnp.var(x, axis=axis, keepdims=True)
    return (x - m) / jnp.sqrt(v + eps)
def _scatter_add(tgt, idx, src, axis=0):
    return tgt.at[idx].add(src)
def _segment_sum(src, seg, n):
    return jax.ops.segment_sum(src, seg, n)

kernel_name = 'mk_rec_standalone_d1_rec_687f8a'

def setup_inputs(seed: int = 0):
    np.random.seed(seed)
    _w = jnp.asarray
    def _rec_inputs():
        import jax
        import jax.numpy as jnp
        _rk = jax.random.key(seed)
        r_x = 1.50771e-05 + 1.00003 * jax.random.normal(jax.random.fold_in(_rk, 1), (16384, 32, 128), jnp.float32)
        return r_x
    r_x = _rec_inputs()
    def _L0_rec_setup():
        import jax, jax.numpy as jnp
        import numpy as np
        N_FEATS = 32
        EMBED_D = 128
        BATCH = 16384
        SELF_INTERACTION = False
        key = jax.random.key(seed)
        x = jax.random.normal(key, (BATCH, N_FEATS, EMBED_D), dtype=jnp.float32)
        return {'x': x}
    _L0_rec_all = _L0_rec_setup()
    _L0_rec_in = {k: v for k, v in _L0_rec_all.items() if k in ()}
    del _L0_rec_all

    return {
        "r_x": r_x,
    }

def reference(r_x):
    import jax
    import jax.numpy as jnp
    def _L0_rec_ref(x):
        import jax, jax.numpy as jnp
        import numpy as np
        N_FEATS = 32
        EMBED_D = 128
        BATCH = 16384
        SELF_INTERACTION = False
        B, N, D = x.shape
        dot = jnp.einsum('bnd,bmd->bnm', x, x)
        k = 0 if SELF_INTERACTION else 1
        iu, ju = jnp.triu_indices(N, k=k)
        flat = dot[:, iu, ju]
        return flat

    y = _L0_rec_ref(r_x)
    return y


_drawn_inputs = setup_inputs


def setup_inputs(seed=0):
    import zlib

    import numpy as np

    out = dict(_drawn_inputs(seed))
    spreads = {}
    factors = {}
    for name, (base, spread) in spreads.items():
        noise = np.random.default_rng([zlib.crc32(name.encode()), seed]).standard_normal(out[name].shape)
        drawn = base * np.exp(spread * noise) if base else spread * noise
        out[name] = jnp.asarray(drawn.astype(out[name].dtype))
    for name, factor in factors.items():
        out[name] = (out[name] * factor).astype(out[name].dtype)
    return out
```

```python
import concourse.bass as bass
from concourse import mybir
from contextlib import ExitStack


BATCH, FEATS, DIM = 16384, 32, 128
PARTITIONS = 128

SAMPLES_PER_TILE = PARTITIONS // FEATS
TILE_COLS = SAMPLES_PER_TILE * FEATS
TILES_PER_UNIT = 16
UNIT_COLS = TILES_PER_UNIT * TILE_COLS
SAMPLES_PER_UNIT = TILES_PER_UNIT * SAMPLES_PER_TILE
UNITS = BATCH // SAMPLES_PER_UNIT
UNITS_PER_GROUP = 16
GROUPS = UNITS // UNITS_PER_GROUP
TILES_PER_GROUP = UNITS_PER_GROUP * TILES_PER_UNIT
RING = 8
HALVES = 2
PACKS = 2
PAIRS = FEATS * (FEATS - 1) // 2
ROWS = FEATS - 1


def row_start(i):
    return sum(FEATS - 1 - r for r in range(i))


def pairwise_dots_kernel(nc: bass.Bass, x_t: bass.AP, out: bass.AP):
    fp32 = mybir.dt.float32
    ctx = ExitStack()
    with ctx:
        def sem(name):
            return ctx.enter_context(nc.semaphore(name))

        x = ctx.enter_context(nc.sbuf_tensor("x", [DIM, RING, UNIT_COLS], fp32))
        scores = ctx.enter_context(nc.psum_tensor("scores", [PARTITIONS, HALVES, UNIT_COLS], fp32))
        packed = ctx.enter_context(nc.sbuf_tensor("packed", [PARTITIONS, PACKS, FEATS - 1, TILES_PER_GROUP], fp32))

        x_loaded = [sem(f"x_loaded{b}") for b in range(RING)]
        scores_ready = [sem(f"scores_ready{h}") for h in range(HALVES)]
        scores_free = [sem(f"scores_free{h}") for h in range(HALVES)]
        stored = [sem(f"stored{b}") for b in range(PACKS)]

        block = ctx.enter_context(nc.Block())

        @block.sync
        def _(sp):
            for b in range(RING):
                sp.dma_start(x[:, b, :], x_t[b]).then_inc(x_loaded[b], 16)
            with sp.Fori(1, UNITS // RING) as turn:
                for b in range(RING):
                    sp.wait_ge(scores_ready[b % HALVES], (turn - 1) * (RING // HALVES) + b // HALVES + 1)
                    sp.dma_start(x[:, b, :], x_t[turn * RING + b]).then_inc(x_loaded[b], 16)

        @block.tensor
        def _(pe):
            with pe.Fori(0, UNITS // RING) as turn:
                for b in range(RING):
                    half = b % HALVES
                    pe.wait_ge(x_loaded[b], turn * 16 + 16)
                    pe.wait_ge(scores_free[half], turn * (RING // HALVES) + b // HALVES + 1)
                    for t in range(TILES_PER_UNIT):
                        cols = x[:, b, t * TILE_COLS:(t + 1) * TILE_COLS]
                        last = nc.tensor.matmul(scores[:, half, t * TILE_COLS:(t + 1) * TILE_COLS], cols, cols,
                                                start=True, stop=True)
                    last.then_inc(scores_ready[half], 1)

        def pack_unit(copy, half, buffer, unit):
            for s in range(SAMPLES_PER_TILE):
                rows = slice(s * FEATS, (s + 1) * FEATS)
                block_of_s = scores[rows, half, :].rearrange("p (t s j) -> p s j t", s=SAMPLES_PER_TILE, j=FEATS)
                last = copy(packed[rows, buffer, :, unit * TILES_PER_UNIT:(unit + 1) * TILES_PER_UNIT],
                            block_of_s[:, s, 1:, :])
            return last

        def pack_groups(eng, copy, half, turn, first):
            for buffer in range(PACKS):
                if not first:
                    eng.wait_ge(stored[buffer], turn * ROWS * 16)
                for n in range(UNITS_PER_GROUP // HALVES):
                    before = turn * (PACKS * UNITS_PER_GROUP // HALVES) + buffer * (UNITS_PER_GROUP // HALVES) + n
                    eng.wait_ge(scores_ready[half], before + 1)
                    last = pack_unit(copy, half, buffer, n * HALVES + half)
                    last.then_inc(scores_free[half], 1)

        @block.scalar
        def _(act):
            act.sem_inc(scores_free[0], 1)
            pack_groups(act, nc.scalar.copy, 0, 0, True)
            with act.Fori(1, GROUPS // PACKS) as turn:
                pack_groups(act, nc.scalar.copy, 0, turn, False)

        @block.vector
        def _(dve):
            dve.sem_inc(scores_free[1], 1)
            pack_groups(dve, nc.vector.tensor_copy, 1, 0, True)
            with dve.Fori(1, GROUPS // PACKS) as turn:
                pack_groups(dve, nc.vector.tensor_copy, 1, turn, False)

        @block.gpsimd
        def _(pool):
            with pool.Fori(0, GROUPS // PACKS) as turn:
                for buffer in range(PACKS):
                    for half in range(HALVES):
                        pool.wait_ge(scores_free[half], (turn * PACKS + buffer + 1) * (UNITS_PER_GROUP // HALVES) + 1)
                    for i in range(ROWS):
                        n = (FEATS - 1 - i) * TILES_PER_GROUP
                        start = SAMPLES_PER_TILE * TILES_PER_GROUP * row_start(i)
                        row = out[turn * PACKS + buffer, start:start + SAMPLES_PER_TILE * n]
                        pool.dma_start(row.rearrange("(s n) -> s n", n=n),
                                       packed[i:PARTITIONS:FEATS, buffer, i:, :].rearrange("s j t -> s (j t)")
                                       ).then_inc(stored[buffer], 16)
            for buffer in range(PACKS):
                pool.wait_ge(stored[buffer], GROUPS // PACKS * ROWS * 16)


def kernel(r_x):
    import numpy as np
    import concourse.bacc as bacc
    from concourse.bass_utils import run_bass_kernel_spmd

    fp32 = mybir.dt.float32
    nc = bacc.Bacc("TRN2", target_bir_lowering=False, num_devices=1)
    x_t = np.ascontiguousarray(np.asarray(r_x).reshape(UNITS, SAMPLES_PER_UNIT * FEATS, DIM).transpose(0, 2, 1))
    out_shape = (GROUPS, PAIRS * SAMPLES_PER_TILE * TILES_PER_GROUP)
    x_dram = nc.dram_tensor("x_t", x_t.shape, fp32, kind="ExternalInput").ap()
    out_dram = nc.dram_tensor("dots", out_shape, fp32, kind="ExternalOutput").ap()
    pairwise_dots_kernel(nc, x_dram, out_dram)
    got = run_bass_kernel_spmd(nc, [{"x_t": x_t}], core_ids=[0]).results[0]["dots"]

    dots = np.empty((GROUPS, TILES_PER_GROUP, SAMPLES_PER_TILE, PAIRS), got.dtype)
    for i in range(ROWS):
        n = FEATS - 1 - i
        start = SAMPLES_PER_TILE * TILES_PER_GROUP * row_start(i)
        row = got[:, start:start + SAMPLES_PER_TILE * n * TILES_PER_GROUP]
        row = row.reshape(GROUPS, SAMPLES_PER_TILE, n, TILES_PER_GROUP)
        dots[:, :, :, row_start(i):row_start(i) + n] = row.transpose(0, 3, 1, 2)
    return dots.reshape(BATCH, PAIRS)
```

```python
import concourse.bass as bass
from concourse import mybir
from contextlib import ExitStack


BATCH, FEATS, DIM = 16384, 32, 128
PARTITIONS = 128
PAIRS = FEATS * (FEATS - 1) // 2
ROWS = FEATS - 1
ABOVE = FEATS - 1

SAMPLES_PER_TILE = PARTITIONS // FEATS
TILE_COLS = SAMPLES_PER_TILE * FEATS
TILES_PER_UNIT = 16
SPLIT = 4
PLAIN = TILES_PER_UNIT - SPLIT
UNIT_COLS = TILES_PER_UNIT * TILE_COLS
SAMPLES_PER_UNIT = TILES_PER_UNIT * SAMPLES_PER_TILE
UNITS = BATCH // SAMPLES_PER_UNIT
RING = 8
HALVES = 2
FIRST_PARTS = 4
UNITS_PER_GROUP = 16
GROUPS = UNITS // UNITS_PER_GROUP
PACKS = 2
TURN = PACKS * UNITS_PER_GROUP
TILES_PER_GROUP = UNITS_PER_GROUP * TILES_PER_UNIT
GROUP_SIZE = PAIRS * SAMPLES_PER_TILE * TILES_PER_GROUP
WHOLE_UNITS = 4
WHOLE_TILES = WHOLE_UNITS * TILES_PER_UNIT
LAST_TILES = TILES_PER_GROUP - WHOLE_TILES
OUT_SIZE = PAIRS * (BATCH - WHOLE_TILES * SAMPLES_PER_TILE)


def row_start(i):
    return sum(FEATS - 1 - r for r in range(i))


def pairwise_dots_kernel(nc: bass.Bass, x_t: bass.AP, out: bass.AP, whole_out: bass.AP):
    fp32, fp32r = mybir.dt.float32, mybir.dt.float32r
    ALU = mybir.AluOpType
    ctx = ExitStack()
    with ctx:
        def sem(name):
            return ctx.enter_context(nc.semaphore(name))

        def sbuf(name, shape, dtype=fp32):
            return ctx.enter_context(nc.sbuf_tensor(name, shape, dtype))

        def psum(name, shape):
            return ctx.enter_context(nc.psum_tensor(name, shape, fp32))

        x = sbuf("x", [DIM, RING, UNIT_COLS])
        parts = sbuf("parts", [DIM, HALVES, SPLIT, 2, TILE_COLS], fp32r)
        plain = psum("plain", [PARTITIONS, HALVES, PLAIN * TILE_COLS])
        split = psum("split", [PARTITIONS, SPLIT, 2, TILE_COLS])
        blocks = sbuf("blocks", [PARTITIONS, HALVES, 2, SPLIT, FEATS])
        turned = sbuf("turned", [PARTITIONS, HALVES, SPLIT, FEATS])
        partial = sbuf("partial", [PARTITIONS, HALVES, SPLIT, FEATS])
        packed = sbuf("packed", [PARTITIONS, PACKS, ABOVE, TILES_PER_GROUP])
        whole = sbuf("whole", [PARTITIONS, ABOVE, WHOLE_TILES])

        x_loaded = [sem(f"x_loaded{b}") for b in range(RING)]
        first_loaded = [sem(f"first_loaded{n}") for n in range(FIRST_PARTS)]
        high_ready = sem("high_ready")
        low_ready = sem("low_ready")
        plain_ready = sem("plain_ready")
        split_ready = sem("split_ready")
        act_copied = sem("act_copied")
        dve_copied = sem("dve_copied")
        split_copied = sem("split_copied")
        terms_ready = sem("terms_ready")
        split_packed = sem("split_packed")
        stored = [sem(f"stored{b}") for b in range(PACKS)]
        sp_stored = sem("sp_stored")
        whole_stored = sem("whole_stored")

        block = ctx.enter_context(nc.Block())

        def products(pe, turn, first):
            for b in range(RING):
                unit = turn * RING + b
                half = b % HALVES
                if not (first and b == 0):
                    pe.wait_ge(x_loaded[b], (turn + (b != 0)) * 16)
                if not first or b >= HALVES:
                    pe.wait_ge(act_copied, unit - HALVES + 1)
                    pe.wait_ge(dve_copied, unit - HALVES + 1)
                for t in range(PLAIN):
                    if first and b == 0 and t % (TILES_PER_UNIT // FIRST_PARTS) == 0:
                        pe.wait_ge(first_loaded[t // (TILES_PER_UNIT // FIRST_PARTS)], 16)
                    cols = slice(t * TILE_COLS, (t + 1) * TILE_COLS)
                    last = nc.tensor.matmul(
                        plain[:, half, cols].rearrange("p (s j) -> p s j", j=FEATS)[:, :, 1:],
                        x[:, b, cols], x[:, b, cols].rearrange("p (s j) -> p s j", j=FEATS)[:, :, 1:],
                        start=True, stop=True)
                last.then_inc(plain_ready, 1)
                pe.wait_ge(low_ready, unit + 1)
                if not first or b >= 1:
                    pe.wait_ge(split_copied, unit)
                for t in range(SPLIT):
                    last = nc.tensor.matmul(split[:, t, :, :], parts[:, half, t, 0, :], parts[:, half, t, :, :],
                                            start=True, stop=True)
                last.then_inc(split_ready, 1)

        @block.tensor
        def _(pe):
            products(pe, 0, True)
            with pe.Fori(1, UNITS // RING) as turn:
                products(pe, turn, False)

        def place(rows, k, last):
            group, n = divmod(k, UNITS_PER_GROUP)
            if last and k >= TURN - WHOLE_UNITS:
                n -= UNITS_PER_GROUP - WHOLE_UNITS
                return whole[rows, :, n * TILES_PER_UNIT:(n + 1) * TILES_PER_UNIT]
            return packed[rows, group, :, n * TILES_PER_UNIT:(n + 1) * TILES_PER_UNIT]

        def pack_plain(copy, samples, k, last_turn):
            for s in samples:
                rows = slice(s * FEATS, (s + 1) * FEATS)
                own = plain[rows, k % HALVES, :].rearrange("p (t s j) -> p s j t", s=SAMPLES_PER_TILE, j=FEATS)
                last = copy(place(rows, k, last_turn)[:, :, 0:PLAIN], own[:, s, 1:, :])
            return last

        def wait_for_pack(eng, turn, k, first):
            if k % UNITS_PER_GROUP == 0 and not first:
                eng.wait_ge(stored[k // UNITS_PER_GROUP], turn * ROWS * 16)

        split_cols = slice(PLAIN * TILE_COLS, UNIT_COLS)
        ACT_SAMPLES, DVE_SAMPLES = (0,), (1, 2, 3)

        def high_parts(act, turn, k, first):
            unit = turn * TURN + k
            b = k % RING
            if first and k == 0:
                act.wait_ge(first_loaded[FIRST_PARTS - 1], 16)
            else:
                act.wait_ge(x_loaded[b], (turn * (TURN // RING) + k // RING + (b != 0)) * 16)
            if not first or k >= HALVES:
                act.wait_ge(split_ready, unit - HALVES + 1)
            nc.scalar.copy(parts[:, k % HALVES, :, 0, :],
                           x[:, b, split_cols].rearrange("p (t c) -> p t c", c=TILE_COLS)).then_inc(high_ready, 1)

        def act_turn(act, turn, first, last):
            for k in range(TURN):
                unit = turn * TURN + k
                if not (last and k == TURN - 1):
                    high_parts(act, turn, k + 1, first)
                wait_for_pack(act, turn, k, first)
                act.wait_ge(plain_ready, unit + 1)
                pack_plain(nc.scalar.copy, ACT_SAMPLES, k, last).then_inc(act_copied, 1)
                act.wait_ge(split_ready, unit + 1)
                if not first or k >= HALVES:
                    act.wait_ge(split_packed, unit - HALVES + 1)
                for s in range(SAMPLES_PER_TILE):
                    rows = slice(s * FEATS, (s + 1) * FEATS)
                    own = split[rows, :, :, s * FEATS:(s + 1) * FEATS].rearrange("p t m j -> p m t j")
                    copied = nc.scalar.copy(blocks[rows, k % HALVES, :, :, :], own)
                copied.then_inc(split_copied, 1)

        @block.scalar
        def _(act):
            high_parts(act, 0, 0, True)
            act_turn(act, 0, True, False)
            with act.Fori(1, UNITS // TURN - 1) as turn:
                act_turn(act, turn, False, False)
            act_turn(act, UNITS // TURN - 1, False, True)
            act.wait_ge(act_copied, UNITS)
            act.wait_ge(split_packed, UNITS)
            act.dma_start(whole_out, whole[:, :, :]).then_inc(whole_stored, 16)
            act.wait_ge(whole_stored, 16)

        def low_parts(dve, turn, k):
            dve.wait_ge(high_ready, turn * TURN + k + 1)
            xs = x[:, k % RING, split_cols].rearrange("p (t c) -> p t c", c=TILE_COLS)
            nc.vector.tensor_tensor(parts[:, k % HALVES, :, 1, :], xs, parts[:, k % HALVES, :, 0, :].bitcast(fp32),
                                    ALU.subtract).then_inc(low_ready, 1)

        def dve_turn(dve, turn, first, last):
            for k in range(TURN):
                unit = turn * TURN + k
                half = k % HALVES
                wait_for_pack(dve, turn, k, first)
                dve.wait_ge(plain_ready, unit + 1)
                pack_plain(nc.vector.tensor_copy, DVE_SAMPLES, k, last).then_inc(dve_copied, 1)
                if not (last and k == TURN - 1):
                    low_parts(dve, turn, k + 1)
                dve.wait_ge(split_copied, unit + 1)
                nc.vector.transpose(turned[:, half, :, :], blocks[:, half, 1, :, :]).then_inc(terms_ready, 1)
                nc.vector.tensor_tensor(partial[:, half, :, :], blocks[:, half, 0, :, :], blocks[:, half, 1, :, :],
                                        ALU.add).then_inc(terms_ready, 1)
                dve.wait_ge(terms_ready, 2 * unit + 2)
                nc.vector.tensor_tensor(place(slice(0, PARTITIONS), k, last)[:, :, PLAIN:],
                                        partial[:, half, :, 1:].rearrange("p t j -> p j t"),
                                        turned[:, half, :, 1:].rearrange("p t j -> p j t"),
                                        ALU.add).then_inc(split_packed, 1)

        @block.vector
        def _(dve):
            low_parts(dve, 0, 0)
            dve_turn(dve, 0, True, False)
            with dve.Fori(1, UNITS // TURN - 1) as turn:
                dve_turn(dve, turn, False, False)
            dve_turn(dve, UNITS // TURN - 1, False, True)

        def store_row(eng, group, buffer, i, tiles):
            n = FEATS - 1 - i
            start = group * GROUP_SIZE + SAMPLES_PER_TILE * tiles * row_start(i)
            row = out[bass.ds(start, SAMPLES_PER_TILE * n * tiles)].rearrange("(s j t) -> s j t", j=n, t=tiles)
            scores = packed[i:PARTITIONS:FEATS, buffer, i:, 0:tiles]
            if tiles == TILES_PER_GROUP:
                return eng.dma_start(row.rearrange("s j t -> s (j t)"), scores.rearrange("s j t -> s (j t)"))
            return eng.dma_start(row, scores)

        def wait_packed(eng, units):
            eng.wait_ge(act_copied, units)
            eng.wait_ge(split_packed, units)

        LAST, LAST_BUFFER = GROUPS - 1, (GROUPS - 1) % PACKS
        SP_ROWS = [i for i in range(ROWS) if i % 5 < 3]
        POOL_ROWS = [i for i in range(ROWS) if i % 5 >= 3]

        @block.sync
        def _(sp):
            for n in range(FIRST_PARTS):
                part = slice(n * UNIT_COLS // FIRST_PARTS, (n + 1) * UNIT_COLS // FIRST_PARTS)
                sp.dma_start(x[:, 0, part], x_t[0, :, part]).then_inc(first_loaded[n], 16)
            for b in range(1, RING):
                sp.dma_start(x[:, b, :], x_t[b]).then_inc(x_loaded[b], 16)
            with sp.Fori(1, UNITS // RING) as turn:
                for b in range(RING):
                    sp.wait_ge(split_ready, (turn - 1) * RING + b + 1)
                    sp.dma_start(x[:, b, :], x_t[turn * RING + b]).then_inc(x_loaded[b], 16)
            wait_packed(sp, UNITS - WHOLE_UNITS)
            for i in SP_ROWS:
                store_row(sp, LAST, LAST_BUFFER, i, LAST_TILES).then_inc(sp_stored, 16)
            sp.wait_ge(sp_stored, 16 * len(SP_ROWS))

        @block.gpsimd
        def _(pool):
            def store_group(group, buffer):
                wait_packed(pool, (group + 1) * UNITS_PER_GROUP)
                for i in range(ROWS):
                    store_row(pool, group, buffer, i, TILES_PER_GROUP).then_inc(stored[buffer], 16)

            with pool.Fori(0, GROUPS // PACKS - 1) as turn:
                for buffer in range(PACKS):
                    store_group(turn * PACKS + buffer, buffer)
            store_group(LAST - 1, 1 - LAST_BUFFER)
            wait_packed(pool, UNITS - WHOLE_UNITS)
            for i in POOL_ROWS:
                store_row(pool, LAST, LAST_BUFFER, i, LAST_TILES).then_inc(stored[LAST_BUFFER], 16)
            pool.wait_ge(stored[1 - LAST_BUFFER], GROUPS // PACKS * ROWS * 16)
            pool.wait_ge(stored[LAST_BUFFER], ((GROUPS // PACKS - 1) * ROWS + len(POOL_ROWS)) * 16)


def kernel(r_x):
    import numpy as np
    import concourse.bacc as bacc
    from concourse.bass_utils import run_bass_kernel_spmd

    fp32 = mybir.dt.float32
    nc = bacc.Bacc("TRN2", target_bir_lowering=False, num_devices=1)
    x_t = np.ascontiguousarray(np.asarray(r_x).reshape(UNITS, SAMPLES_PER_UNIT * FEATS, DIM).transpose(0, 2, 1))
    x_dram = nc.dram_tensor("x_t", x_t.shape, fp32, kind="ExternalInput").ap()
    out_dram = nc.dram_tensor("dots", (OUT_SIZE,), fp32, kind="ExternalOutput").ap()
    whole_dram = nc.dram_tensor("whole_dots", (PARTITIONS, ABOVE, WHOLE_TILES), fp32, kind="ExternalOutput").ap()
    pairwise_dots_kernel(nc, x_dram, out_dram, whole_dram)
    got = run_bass_kernel_spmd(nc, [{"x_t": x_t}], core_ids=[0]).results[0]
    rows, whole = got["dots"], got["whole_dots"].reshape(SAMPLES_PER_TILE, FEATS, ABOVE, WHOLE_TILES)

    dots = np.empty((BATCH // SAMPLES_PER_TILE, SAMPLES_PER_TILE, PAIRS), rows.dtype)
    by_rows = (GROUPS - 1) * TILES_PER_GROUP + LAST_TILES
    for i in range(ROWS):
        n = FEATS - 1 - i
        pairs = slice(row_start(i), row_start(i) + n)
        for first in range(0, by_rows, TILES_PER_GROUP):
            tiles = min(TILES_PER_GROUP, by_rows - first)
            start = first * SAMPLES_PER_TILE * PAIRS + SAMPLES_PER_TILE * tiles * row_start(i)
            row = rows[start:start + SAMPLES_PER_TILE * n * tiles].reshape(SAMPLES_PER_TILE, n, tiles)
            dots[first:first + tiles, :, pairs] = row.transpose(2, 0, 1)
        dots[by_rows:, :, pairs] = whole[:, i, i:, :].transpose(2, 0, 1)
    return dots.reshape(BATCH, PAIRS)
```

```python
import concourse.bass as bass
from concourse import mybir
from contextlib import ExitStack


BATCH, FEATS, DIM = 16384, 32, 128
PARTITIONS = 128
PAIRS = FEATS * (FEATS - 1) // 2
ROWS = FEATS - 1
ABOVE = FEATS - 1
USED = PARTITIONS - 1

SAMPLES_PER_TILE = PARTITIONS // FEATS
TILE_COLS = SAMPLES_PER_TILE * FEATS
TILES_PER_UNIT = 16
SPLIT = 4
PLAIN = TILES_PER_UNIT - SPLIT
TILES_PER_BANK = 2
UNIT_COLS = TILES_PER_UNIT * TILE_COLS
SAMPLES_PER_UNIT = TILES_PER_UNIT * SAMPLES_PER_TILE
UNITS = BATCH // SAMPLES_PER_UNIT
RING = 8
HALVES = 2
FIRST_PARTS = 4
UNITS_PER_GROUP = 16
GROUPS = UNITS // UNITS_PER_GROUP
PACKS = 2
TURN = PACKS * UNITS_PER_GROUP
TILES_PER_GROUP = UNITS_PER_GROUP * TILES_PER_UNIT
GROUP_SIZE = PAIRS * SAMPLES_PER_TILE * TILES_PER_GROUP
WHOLE_UNITS = 5
WHOLE_TILES = WHOLE_UNITS * TILES_PER_UNIT
LAST_TILES = TILES_PER_GROUP - WHOLE_TILES
OUT_SIZE = PAIRS * (BATCH - WHOLE_TILES * SAMPLES_PER_TILE)


def row_start(i):
    return sum(FEATS - 1 - r for r in range(i))


def pairwise_dots_kernel(nc: bass.Bass, x_t: bass.AP, out: bass.AP, whole_out: bass.AP):
    fp32, fp32r, bf16 = mybir.dt.float32, mybir.dt.float32r, mybir.dt.bfloat16
    ALU = mybir.AluOpType
    ctx = ExitStack()
    with ctx:
        def sem(name):
            return ctx.enter_context(nc.semaphore(name))

        def sbuf(name, shape, dtype=fp32):
            return ctx.enter_context(nc.sbuf_tensor(name, shape, dtype))

        def psum(name, shape):
            return ctx.enter_context(nc.psum_tensor(name, shape, fp32))

        x = sbuf("x", [DIM, RING, UNIT_COLS])
        parts = sbuf("parts", [DIM, HALVES, SPLIT, 2, TILE_COLS], fp32r)
        lows = sbuf("lows", [DIM, HALVES, SPLIT, TILE_COLS], bf16)
        plain = psum("plain", [PARTITIONS, HALVES, PLAIN * TILE_COLS])
        split = psum("split", [PARTITIONS, SPLIT, 2, TILE_COLS])
        blocks = sbuf("blocks", [PARTITIONS, HALVES, 2, SPLIT, FEATS])
        turned = sbuf("turned", [PARTITIONS, HALVES, SPLIT, FEATS])
        partial = sbuf("partial", [PARTITIONS, HALVES, SPLIT, FEATS])
        packed = sbuf("packed", [PARTITIONS, PACKS, ABOVE, TILES_PER_GROUP])
        whole = sbuf("whole", [PARTITIONS, WHOLE_UNITS, ABOVE, TILES_PER_UNIT])

        x_loaded = [sem(f"x_loaded{b}") for b in range(RING)]
        first_loaded = [sem(f"first_loaded{n}") for n in range(FIRST_PARTS)]
        plain_cleared = sem("plain_cleared")
        high_ready = sem("high_ready")
        low_ready = sem("low_ready")
        lows_ready = sem("lows_ready")
        plain_ready = sem("plain_ready")
        split_ready = sem("split_ready")
        act_copied = sem("act_copied")
        dve_copied = sem("dve_copied")
        split_copied = sem("split_copied")
        terms_ready = sem("terms_ready")
        split_packed = sem("split_packed")
        stored = [sem(f"stored{b}") for b in range(PACKS)]
        sp_stored = sem("sp_stored")
        whole_stored = [sem(f"whole_stored{n}") for n in range(WHOLE_UNITS)]

        block = ctx.enter_context(nc.Block())

        def products(pe, turn, first):
            for b in range(RING):
                unit = turn * RING + b
                half = b % HALVES
                if not (first and b == 0):
                    pe.wait_ge(x_loaded[b], (turn + (b != 0)) * 16)
                if first and b < HALVES:
                    pe.wait_ge(plain_cleared, b + 1)
                else:
                    pe.wait_ge(act_copied, unit - HALVES + 1)
                    pe.wait_ge(dve_copied, unit - HALVES + 1)
                for t in range(PLAIN):
                    if first and b == 0 and t % (TILES_PER_UNIT // FIRST_PARTS) == 0:
                        pe.wait_ge(first_loaded[t // (TILES_PER_UNIT // FIRST_PARTS)], 16)
                    cols = slice(t * TILE_COLS, (t + 1) * TILE_COLS)
                    last = nc.tensor.matmul(
                        plain[0:USED, half, cols].rearrange("p (s j) -> p s j", j=FEATS)[:, :, 1:],
                        x[:, b, t * TILE_COLS:t * TILE_COLS + USED],
                        x[:, b, cols].rearrange("p (s j) -> p s j", j=FEATS)[:, :, 1:],
                        start=True, stop=True)
                last.then_inc(plain_ready, 1)
                pe.wait_ge(low_ready, unit + 1)
                pe.wait_ge(lows_ready, unit + 1)
                if not first or b >= 1:
                    pe.wait_ge(split_copied, unit)
                for t in range(SPLIT):
                    nc.tensor.matmul(split[:, t, :, :], parts[:, half, t, 0, :], parts[:, half, t, :, :],
                                     start=t % TILES_PER_BANK == 0, stop=False, skip_group_check=True)
                for t in range(SPLIT):
                    last = nc.tensor.matmul(
                        split[:, t, 0, :].rearrange("p (s j) -> p s j", j=FEATS)[:, :, 1:],
                        lows[:, half, t, :], lows[:, half, t, :].rearrange("p (s j) -> p s j", j=FEATS)[:, :, 1:],
                        start=False, stop=True, skip_group_check=True)
                last.then_inc(split_ready, 1)

        @block.tensor
        def _(pe):
            products(pe, 0, True)
            with pe.Fori(1, UNITS // RING) as turn:
                products(pe, turn, False)

        def place(rows, k, last):
            group, n = divmod(k, UNITS_PER_GROUP)
            if last and k >= TURN - WHOLE_UNITS:
                return whole[rows, n - (UNITS_PER_GROUP - WHOLE_UNITS), :, :]
            return packed[rows, group, :, n * TILES_PER_UNIT:(n + 1) * TILES_PER_UNIT]

        def pack_plain(copy, samples, k, last_turn):
            for s in samples:
                rows = slice(s * FEATS, (s + 1) * FEATS)
                own = plain[rows, k % HALVES, :].rearrange("p (t s j) -> p s j t", s=SAMPLES_PER_TILE, j=FEATS)
                last = copy(place(rows, k, last_turn)[:, :, 0:PLAIN], own[:, s, 1:, :])
            return last

        def wait_for_pack(eng, turn, k, first):
            if k % UNITS_PER_GROUP == 0 and not first:
                eng.wait_ge(stored[k // UNITS_PER_GROUP], turn * ROWS * 16)

        split_cols = slice(PLAIN * TILE_COLS, UNIT_COLS)

        def act_share(k, last):
            return 2 if last and k == TURN - 1 else 1

        def high_parts(act, turn, k, first):
            unit = turn * TURN + k
            b = k % RING
            if first and k == 0:
                act.wait_ge(first_loaded[FIRST_PARTS - 1], 16)
            else:
                act.wait_ge(x_loaded[b], (turn * (TURN // RING) + k // RING + (b != 0)) * 16)
            if not first or k >= HALVES:
                act.wait_ge(split_ready, unit - HALVES + 1)
            nc.scalar.copy(parts[:, k % HALVES, :, 0, :],
                           x[:, b, split_cols].rearrange("p (t c) -> p t c", c=TILE_COLS)).then_inc(high_ready, 1)

        def low_copies(act, turn, k):
            act.wait_ge(low_ready, turn * TURN + k + 1)
            nc.scalar.copy(lows[:, k % HALVES, :, :],
                           parts[:, k % HALVES, :, 1, :].bitcast(fp32)).then_inc(lows_ready, 1)

        def act_turn(act, turn, first, last):
            for k in range(TURN):
                unit = turn * TURN + k
                if not (last and k == TURN - 1):
                    high_parts(act, turn, k + 1, first)
                wait_for_pack(act, turn, k, first)
                act.wait_ge(plain_ready, unit + 1)
                pack_plain(nc.scalar.copy, range(act_share(k, last)), k, last).then_inc(act_copied, 1)
                act.wait_ge(split_ready, unit + 1)
                if not first or k >= HALVES:
                    act.wait_ge(split_packed, unit - HALVES + 1)
                for s in range(SAMPLES_PER_TILE):
                    rows = slice(s * FEATS, (s + 1) * FEATS)
                    own = split[rows, :, :, s * FEATS:(s + 1) * FEATS].rearrange("p t m j -> p m t j")
                    copied = nc.scalar.copy(blocks[rows, k % HALVES, :, :, :], own)
                copied.then_inc(split_copied, 1)
                if not (last and k == TURN - 1):
                    low_copies(act, turn, k + 1)

        @block.scalar
        def _(act):
            high_parts(act, 0, 0, True)
            low_copies(act, 0, 0)
            act_turn(act, 0, True, False)
            with act.Fori(1, UNITS // TURN - 1) as turn:
                act_turn(act, turn, False, False)
            act_turn(act, UNITS // TURN - 1, False, True)

        def low_parts(dve, turn, k):
            dve.wait_ge(high_ready, turn * TURN + k + 1)
            xs = x[:, k % RING, split_cols].rearrange("p (t c) -> p t c", c=TILE_COLS)
            nc.vector.tensor_tensor(parts[:, k % HALVES, :, 1, :], xs, parts[:, k % HALVES, :, 0, :].bitcast(fp32),
                                    ALU.subtract).then_inc(low_ready, 1)

        def dve_turn(dve, turn, first, last):
            for k in range(TURN):
                unit = turn * TURN + k
                half = k % HALVES
                if not (last and k == TURN - 1):
                    low_parts(dve, turn, k + 1)
                wait_for_pack(dve, turn, k, first)
                dve.wait_ge(plain_ready, unit + 1)
                pack_plain(nc.vector.tensor_copy, range(act_share(k, last), SAMPLES_PER_TILE), k,
                           last).then_inc(dve_copied, 1)
                dve.wait_ge(split_copied, unit + 1)
                nc.vector.transpose(turned[:, half, :, :], blocks[:, half, 1, :, :]).then_inc(terms_ready, 1)
                nc.vector.tensor_tensor(partial[:, half, :, :], blocks[:, half, 0, :, :], blocks[:, half, 1, :, :],
                                        ALU.add).then_inc(terms_ready, 1)
                dve.wait_ge(terms_ready, 2 * unit + 2)
                nc.vector.tensor_tensor(place(slice(0, PARTITIONS), k, last)[:, :, PLAIN:],
                                        partial[:, half, :, 1:].rearrange("p t j -> p j t"),
                                        turned[:, half, :, 1:].rearrange("p t j -> p j t"),
                                        ALU.add).then_inc(split_packed, 1)

        @block.vector
        def _(dve):
            for half in range(HALVES):
                nc.vector.memset(plain[PARTITIONS - FEATS:PARTITIONS, half, :], 0.0).then_inc(plain_cleared, 1)
            low_parts(dve, 0, 0)
            dve_turn(dve, 0, True, False)
            with dve.Fori(1, UNITS // TURN - 1) as turn:
                dve_turn(dve, turn, False, False)
            dve_turn(dve, UNITS // TURN - 1, False, True)

        def store_row(eng, group, buffer, i, tiles):
            n = FEATS - 1 - i
            start = group * GROUP_SIZE + SAMPLES_PER_TILE * tiles * row_start(i)
            row = out[bass.ds(start, SAMPLES_PER_TILE * n * tiles)].rearrange("(s j t) -> s j t", j=n, t=tiles)
            scores = packed[i:PARTITIONS:FEATS, buffer, i:, 0:tiles]
            if tiles == TILES_PER_GROUP:
                return eng.dma_start(row.rearrange("s j t -> s (j t)"), scores.rearrange("s j t -> s (j t)"))
            return eng.dma_start(row, scores)

        def wait_packed(eng, units):
            eng.wait_ge(act_copied, units)
            eng.wait_ge(split_packed, units)

        LAST, LAST_BUFFER = GROUPS - 1, (GROUPS - 1) % PACKS
        SP_ROWS = [i for i in range(ROWS) if i % 5 < 3]
        POOL_ROWS = [i for i in range(ROWS) if i % 5 >= 3]

        @block.sync
        def _(sp):
            for n in range(FIRST_PARTS):
                part = slice(n * UNIT_COLS // FIRST_PARTS, (n + 1) * UNIT_COLS // FIRST_PARTS)
                sp.dma_start(x[:, 0, part], x_t[0, :, part]).then_inc(first_loaded[n], 16)
            for b in range(1, RING):
                sp.dma_start(x[:, b, :], x_t[b]).then_inc(x_loaded[b], 16)
            with sp.Fori(1, UNITS // RING) as turn:
                for b in range(RING):
                    sp.wait_ge(split_ready, (turn - 1) * RING + b + 1)
                    sp.dma_start(x[:, b, :], x_t[turn * RING + b]).then_inc(x_loaded[b], 16)
            wait_packed(sp, UNITS - WHOLE_UNITS)
            for i in SP_ROWS:
                store_row(sp, LAST, LAST_BUFFER, i, LAST_TILES).then_inc(sp_stored, 16)
            for n in range(WHOLE_UNITS):
                wait_packed(sp, UNITS - WHOLE_UNITS + n + 1)
                sp.dma_start(whole_out[n], whole[:, n, :, :]).then_inc(whole_stored[n], 16)
            sp.wait_ge(sp_stored, 16 * len(SP_ROWS))
            for n in range(WHOLE_UNITS):
                sp.wait_ge(whole_stored[n], 16)

        @block.gpsimd
        def _(pool):
            def store_group(group, buffer):
                wait_packed(pool, (group + 1) * UNITS_PER_GROUP)
                for i in range(ROWS):
                    store_row(pool, group, buffer, i, TILES_PER_GROUP).then_inc(stored[buffer], 16)

            with pool.Fori(0, GROUPS // PACKS - 1) as turn:
                for buffer in range(PACKS):
                    store_group(turn * PACKS + buffer, buffer)
            store_group(LAST - 1, 1 - LAST_BUFFER)
            wait_packed(pool, UNITS - WHOLE_UNITS)
            for i in POOL_ROWS:
                store_row(pool, LAST, LAST_BUFFER, i, LAST_TILES).then_inc(stored[LAST_BUFFER], 16)
            pool.wait_ge(stored[1 - LAST_BUFFER], GROUPS // PACKS * ROWS * 16)
            pool.wait_ge(stored[LAST_BUFFER], ((GROUPS // PACKS - 1) * ROWS + len(POOL_ROWS)) * 16)


def kernel(r_x):
    import numpy as np
    import concourse.bacc as bacc
    from concourse.bass_utils import run_bass_kernel_spmd

    fp32 = mybir.dt.float32
    nc = bacc.Bacc("TRN2", target_bir_lowering=False, num_devices=1)
    x_t = np.ascontiguousarray(np.asarray(r_x).reshape(UNITS, SAMPLES_PER_UNIT * FEATS, DIM).transpose(0, 2, 1))
    x_dram = nc.dram_tensor("x_t", x_t.shape, fp32, kind="ExternalInput").ap()
    out_dram = nc.dram_tensor("dots", (OUT_SIZE,), fp32, kind="ExternalOutput").ap()
    whole_shape = (WHOLE_UNITS, PARTITIONS, ABOVE, TILES_PER_UNIT)
    whole_dram = nc.dram_tensor("whole_dots", whole_shape, fp32, kind="ExternalOutput").ap()
    pairwise_dots_kernel(nc, x_dram, out_dram, whole_dram)
    got = run_bass_kernel_spmd(nc, [{"x_t": x_t}], core_ids=[0]).results[0]
    rows = got["dots"]
    whole = got["whole_dots"].reshape(WHOLE_UNITS, SAMPLES_PER_TILE, FEATS, ABOVE, TILES_PER_UNIT)

    dots = np.empty((BATCH // SAMPLES_PER_TILE, SAMPLES_PER_TILE, PAIRS), rows.dtype)
    by_rows = (GROUPS - 1) * TILES_PER_GROUP + LAST_TILES
    for i in range(ROWS):
        n = FEATS - 1 - i
        pairs = slice(row_start(i), row_start(i) + n)
        for first in range(0, by_rows, TILES_PER_GROUP):
            tiles = min(TILES_PER_GROUP, by_rows - first)
            start = first * SAMPLES_PER_TILE * PAIRS + SAMPLES_PER_TILE * tiles * row_start(i)
            row = rows[start:start + SAMPLES_PER_TILE * n * tiles].reshape(SAMPLES_PER_TILE, n, tiles)
            dots[first:first + tiles, :, pairs] = row.transpose(2, 0, 1)
        dots[by_rows:, :, pairs] = whole[:, :, i, i:, :].transpose(0, 3, 1, 2).reshape(-1, SAMPLES_PER_TILE, n)
    return dots.reshape(BATCH, PAIRS)
```
